# Optimizing a Trainium2 kernel written in Bass

```python
import numpy as np
import jax
import jax.numpy as jnp

def _softmax(x, axis=-1):
    return jax.nn.softmax(x, axis=axis)
def _gelu(x):
    return jax.nn.gelu(x, approximate=True)
def _silu(x):
    return jax.nn.silu(x)
def _sigmoid(x):
    return jax.nn.sigmoid(x)
def _layernorm(x, axis=-1, eps=1e-5):
    m = jnp.mean(x, axis=axis, keepdims=True)
    v = jnp.var(x, axis=axis, keepdims=True)
    return (x - m) / jnp.sqrt(v + eps)
def _scatter_add(tgt, idx, src, axis=0):
    return tgt.at[idx].add(src)
def _segment_sum(src, seg, n):
    return jax.ops.segment_sum(src, seg, n)

kernel_name = 'mk_vit_tower_d1_tok_img256_98533d'

def setup_inputs(seed: int = 0):
    np.random.seed(seed)
    _w = jnp.asarray
    def _rec_inputs():
        import jax
        import jax.numpy as jnp
        _rk = jax.random.key(seed)
        x = (-0.000125008 + 0.999885 * jax.random.normal(jax.random.fold_in(_rk, 1), (16, 256, 128, 128), jnp.float32))
        return x
    x = _rec_inputs()
    def _L0_tok_setup():
        import jax, jax.numpy as jnp
        import numpy as np
        D_MODEL = 256
        NHEAD = 8
        DS = 4
        OFFSET_SCALE = 4.0

        def bilinear_sample(fm, pts):
            B, C, H, W = fm.shape
            x = (pts[..., 0] + 1.0) * 0.5 * (W - 1)
            y = (pts[..., 1] + 1.0) * 0.5 * (H - 1)
            x0 = jnp.clip(jnp.floor(x), 0.0, W - 2)
            y0 = jnp.clip(jnp.floor(y), 0.0, H - 2)
            wx = jnp.clip(x - x0, 0.0, 1.0)
            wy = jnp.clip(y - y0, 0.0, 1.0)
            x0i = x0.astype(jnp.int32)
            y0i = y0.astype(jnp.int32)
            fm2 = fm.reshape(B, C, H * W)
            N, P = (pts.shape[1], pts.shape[2])

            def gather(yi, xi):
                idx = (yi * W + xi).reshape(B, N * P)
                g = jnp.take_along_axis(fm2, idx[:, None, :], axis=2)
                return g.reshape(B, C, N, P)
            v00 = gather(y0i, x0i)
            v01 = gather(y0i, x0i + 1)
            v10 = gather(y0i + 1, x0i)
            v11 = gather(y0i + 1, x0i + 1)
            wx_ = wx[:, None]
            wy_ = wy[:, None]
            out = v00 * (1 - wx_) * (1 - wy_) + v01 * wx_ * (1 - wy_) + v10 * (1 - wx_) * wy_ + v11 * wx_ * wy_
            return jnp.moveaxis(out, 1, -1)

        def layer_norm(x, g, b, eps=1e-05):
            mu = jnp.mean(x, axis=-1, keepdims=True)
            var = jnp.var(x, axis=-1, keepdims=True)
            return (x - mu) * jax.lax.rsqrt(var + eps) * g + b

        def reference_points(B, H, W):
            yc = jnp.linspace(-1.0, 1.0, H // DS)
            xc = jnp.linspace(-1.0, 1.0, W // DS)
            yg, xg = jnp.meshgrid(yc, xc, indexing='ij')
            ref = jnp.stack([xg.reshape(-1), yg.reshape(-1)], axis=-1)
            return jnp.broadcast_to(ref[None], (B,) + ref.shape)
        key = jax.random.key(seed)
        ks = jax.random.split(key, 6)
        B, C, H, W = (8, D_MODEL, 128, 128)
        s = 0.05
        return {'feature_map': jax.random.normal(ks[0], (B, C, H, W), jnp.float32), 'W_q': jax.random.normal(ks[1], (C, C), jnp.float32) * s, 'W_k': jax.random.normal(ks[2], (C, C), jnp.float32) * s, 'W_v': jax.random.normal(ks[3], (C, C), jnp.float32) * s, 'W_o1': jax.random.normal(ks[4], (C, C // DS), jnp.float32) * s, 'b_o1': jnp.zeros((C // DS,), jnp.float32), 'ln_g': jnp.ones((C // DS,), jnp.float32), 'ln_b': jnp.zeros((C // DS,), jnp.float32), 'W_o2': jax.random.normal(ks[5], (C // DS, NHEAD * 2), jnp.float32) * s, 'b_o2': jnp.zeros((NHEAD * 2,), jnp.float32)}
    _L0_tok_all = _L0_tok_setup()
    _L0_tok_in = {k: v for k, v in _L0_tok_all.items() if k in ('W_q', 'W_k', 'W_v', 'W_o1', 'b_o1', 'ln_g', 'ln_b', 'W_o2', 'b_o2', )}
    del _L0_tok_all

    def _L0_attn_setup():
        import jax, jax.numpy as jnp
        import numpy as np
        B, N, C, H = (8, 16384, 256, 8)
        D = C // H
        GH = C // 4
        key = jax.random.key(seed)
        ks = jax.random.split(key, 6)
        s = 0.02
        return {'x': jax.random.normal(ks[0], (B, N, C), dtype=jnp.float32), 'Wqkv': jax.random.normal(ks[1], (C, 3 * C), dtype=jnp.float32) * s, 'Wproj': jax.random.normal(ks[2], (C, C), dtype=jnp.float32) * s, 'bproj': jnp.zeros((C,), dtype=jnp.float32), 'ln_g': jnp.ones((C,), dtype=jnp.float32), 'ln_b': jnp.zeros((C,), dtype=jnp.float32), 'Wg1': jax.random.normal(ks[3], (C, GH), dtype=jnp.float32) * s, 'bg1': jnp.zeros((GH,), dtype=jnp.float32), 'Wg2': jax.random.normal(ks[4], (GH, C), dtype=jnp.float32) * s, 'bg2': jnp.zeros((C,), dtype=jnp.float32)}
    _L0_attn_all = _L0_attn_setup()
    _L0_attn_in = {k: v for k, v in _L0_attn_all.items() if k in ('Wqkv', 'Wproj', 'bproj', 'ln_g', 'ln_b', 'Wg1', 'bg1', 'Wg2', 'bg2', )}
    del _L0_attn_all

    def _L0_ffn_setup():
        import jax, jax.numpy as jnp
        import numpy as np
        B, S, D = (8, 4096, 256)
        H = 4 * D
        CAPACITY = 0.5
        key = jax.random.key(seed)
        ks = jax.random.split(key, 6)
        x = jax.random.normal(ks[0], (B, S, D), dtype=jnp.float32)
        attention_mask = jnp.zeros((B, 1, 1, S), dtype=jnp.float32)
        wr = jax.random.normal(ks[1], (D, 1), dtype=jnp.float32) * 0.02
        br = jnp.zeros((1,), dtype=jnp.float32)
        w1 = jax.random.normal(ks[2], (D, H), dtype=jnp.float32) * 0.02
        b1 = jnp.zeros((H,), dtype=jnp.float32)
        w2 = jax.random.normal(ks[3], (H, D), dtype=jnp.float32) * 0.02
        b2 = jnp.zeros((D,), dtype=jnp.float32)
        return {'x': x, 'attention_mask': attention_mask, 'wr': wr, 'br': br, 'w1': w1, 'b1': b1, 'w2': w2, 'b2': b2}
    _L0_ffn_all = _L0_ffn_setup()
    _L0_ffn_in = {k: v for k, v in _L0_ffn_all.items() if k in ('attention_mask', 'wr', 'br', 'w1', 'b1', 'w2', 'b2', )}
    del _L0_ffn_all

    return {
        "x": x,
        "L0_tok_W_q": _L0_tok_in["W_q"],
        "L0_tok_W_k": _L0_tok_in["W_k"],
        "L0_tok_W_v": _L0_tok_in["W_v"],
        "L0_tok_W_o1": _L0_tok_in["W_o1"],
        "L0_tok_b_o1": _L0_tok_in["b_o1"],
        "L0_tok_ln_g": _L0_tok_in["ln_g"],
        "L0_tok_ln_b": _L0_tok_in["ln_b"],
        "L0_tok_W_o2": _L0_tok_in["W_o2"],
        "L0_tok_b_o2": _L0_tok_in["b_o2"],
        "L0_attn_Wqkv": _L0_attn_in["Wqkv"],
        "L0_attn_Wproj": _L0_attn_in["Wproj"],
        "L0_attn_bproj": _L0_attn_in["bproj"],
        "L0_attn_ln_g": _L0_attn_in["ln_g"],
        "L0_attn_ln_b": _L0_attn_in["ln_b"],
        "L0_attn_Wg1": _L0_attn_in["Wg1"],
        "L0_attn_bg1": _L0_attn_in["bg1"],
        "L0_attn_Wg2": _L0_attn_in["Wg2"],
        "L0_attn_bg2": _L0_attn_in["bg2"],
        "L0_ffn_attention_mask": _L0_ffn_in["attention_mask"],
        "L0_ffn_wr": _L0_ffn_in["wr"],
        "L0_ffn_br": _L0_ffn_in["br"],
        "L0_ffn_w1": _L0_ffn_in["w1"],
        "L0_ffn_b1": _L0_ffn_in["b1"],
        "L0_ffn_w2": _L0_ffn_in["w2"],
        "L0_ffn_b2": _L0_ffn_in["b2"],
    }

def reference(x, L0_tok_W_q, L0_tok_W_k, L0_tok_W_v, L0_tok_W_o1, L0_tok_b_o1, L0_tok_ln_g, L0_tok_ln_b, L0_tok_W_o2, L0_tok_b_o2, L0_attn_Wqkv, L0_attn_Wproj, L0_attn_bproj, L0_attn_ln_g, L0_attn_ln_b, L0_attn_Wg1, L0_attn_bg1, L0_attn_Wg2, L0_attn_bg2, L0_ffn_attention_mask, L0_ffn_wr, L0_ffn_br, L0_ffn_w1, L0_ffn_b1, L0_ffn_w2, L0_ffn_b2):
    import jax
    import jax.numpy as jnp
    def _L0_tok_ref(feature_map, W_q, W_k, W_v, W_o1, b_o1, ln_g, ln_b, W_o2, b_o2):
        import jax, jax.numpy as jnp
        import numpy as np
        D_MODEL = 256
        NHEAD = 8
        DS = 4
        OFFSET_SCALE = 4.0

        def bilinear_sample(fm, pts):
            B, C, H, W = fm.shape
            x = (pts[..., 0] + 1.0) * 0.5 * (W - 1)
            y = (pts[..., 1] + 1.0) * 0.5 * (H - 1)
            x0 = jnp.clip(jnp.floor(x), 0.0, W - 2)
            y0 = jnp.clip(jnp.floor(y), 0.0, H - 2)
            wx = jnp.clip(x - x0, 0.0, 1.0)
            wy = jnp.clip(y - y0, 0.0, 1.0)
            x0i = x0.astype(jnp.int32)
            y0i = y0.astype(jnp.int32)
            fm2 = fm.reshape(B, C, H * W)
            N, P = (pts.shape[1], pts.shape[2])

            def gather(yi, xi):
                idx = (yi * W + xi).reshape(B, N * P)
                g = jnp.take_along_axis(fm2, idx[:, None, :], axis=2)
                return g.reshape(B, C, N, P)
            v00 = gather(y0i, x0i)
            v01 = gather(y0i, x0i + 1)
            v10 = gather(y0i + 1, x0i)
            v11 = gather(y0i + 1, x0i + 1)
            wx_ = wx[:, None]
            wy_ = wy[:, None]
            out = v00 * (1 - wx_) * (1 - wy_) + v01 * wx_ * (1 - wy_) + v10 * (1 - wx_) * wy_ + v11 * wx_ * wy_
            return jnp.moveaxis(out, 1, -1)

        def layer_norm(x, g, b, eps=1e-05):
            mu = jnp.mean(x, axis=-1, keepdims=True)
            var = jnp.var(x, axis=-1, keepdims=True)
            return (x - mu) * jax.lax.rsqrt(var + eps) * g + b

        def reference_points(B, H, W):
            yc = jnp.linspace(-1.0, 1.0, H // DS)
            xc = jnp.linspace(-1.0, 1.0, W // DS)
            yg, xg = jnp.meshgrid(yc, xc, indexing='ij')
            ref = jnp.stack([xg.reshape(-1), yg.reshape(-1)], axis=-1)
            return jnp.broadcast_to(ref[None], (B,) + ref.shape)
        B, C, H, W = feature_map.shape
        dh = C // NHEAD
        ref = reference_points(B, H, W)
        Nq = ref.shape[1]
        q_feat = bilinear_sample(feature_map, ref[:, :, None, :])[:, :, 0]
        queries = q_feat @ W_q.T
        h = jax.nn.gelu(layer_norm(q_feat @ W_o1 + b_o1, ln_g, ln_b))
        off = (h @ W_o2 + b_o2).reshape(B, Nq, NHEAD, 2) * OFFSET_SCALE
        scale = jnp.array([2.0 / (W - 1), 2.0 / (H - 1)], jnp.float32)
        sampling_points = ref[:, :, None, :] + off * scale
        sampled = bilinear_sample(feature_map, sampling_points)
        keys = jnp.einsum('bnpc,dc->bnpd', sampled, W_k)
        values = jnp.einsum('bnpc,dc->bnpd', sampled, W_v)
        q = queries.reshape(B, Nq, NHEAD, dh)
        k = keys.reshape(B, Nq, NHEAD, NHEAD, dh)
        v = values.reshape(B, Nq, NHEAD, NHEAD, dh)
        scores = jnp.einsum('bnhd,bnphd->bnhp', q, k) / jnp.sqrt(jnp.float32(dh))
        attn = jax.nn.softmax(scores, axis=-1)
        out = jnp.einsum('bnhp,bnphd->bnhd', attn, v).reshape(B, Nq, C)
        return out

    def _L0_attn_ref(x, Wqkv, Wproj, bproj, ln_g, ln_b, Wg1, bg1, Wg2, bg2):
        import jax, jax.numpy as jnp
        import numpy as np
        B, N, C, H = (8, 16384, 256, 8)
        D = C // H
        GH = C // 4
        b, n, c = x.shape
        h, d = (H, D)
        qkv = (x @ Wqkv).reshape(b, n, 3, h, d)
        q, k, v = (qkv[:, :, 0], qkv[:, :, 1], qkv[:, :, 2])
        k = jax.nn.softmax(k, axis=1)
        context = jnp.einsum('bnhd,bnhv->bhdv', k, v)
        out = jnp.einsum('bnhd,bhdv->bnhv', q, context).reshape(b, n, c)
        mu = jnp.mean(x, axis=-1, keepdims=True)
        var = jnp.var(x, axis=-1, keepdims=True)
        xn = (x - mu) * jax.lax.rsqrt(var + 1e-05) * ln_g + ln_b
        hgate = jax.nn.gelu(xn @ Wg1 + bg1, approximate=False)
        gate = jax.nn.sigmoid(hgate @ Wg2 + bg2)
        return out * gate @ Wproj + bproj

    def _L0_ffn_ref(x, attention_mask, wr, br, w1, b1, w2, b2):
        import jax, jax.numpy as jnp
        import numpy as np
        B, S, D = (8, 4096, 256)
        H = 4 * D
        CAPACITY = 0.5
        b, s, d = x.shape
        weights = (jnp.einsum('bsd,do->bso', x, wr) + br)[..., 0]
        k = max(1, int(CAPACITY * s))
        kk = k - 1 if k > 1 else 1
        _, idx = jax.lax.top_k(weights, k)
        sel_idx = idx[:, :kk]
        sel = jnp.take_along_axis(x, sel_idx[:, :, None], axis=1)
        h = jax.nn.gelu(jnp.einsum('bkd,dh->bkh', sel, w1) + b1)
        y = jnp.einsum('bkh,hd->bkd', h, w2) + b2
        w_sel = jnp.take_along_axis(weights, sel_idx, axis=1)
        y = y * w_sel[..., None]
        batch_idx = jnp.arange(b)[:, None]
        processed = jnp.zeros_like(x).at[batch_idx, sel_idx].set(y)
        return processed + x

    h = _L0_tok_ref(x, L0_tok_W_q, L0_tok_W_k, L0_tok_W_v, L0_tok_W_o1, L0_tok_b_o1, L0_tok_ln_g, L0_tok_ln_b, L0_tok_W_o2, L0_tok_b_o2)
    h = h + _L0_attn_ref(_layernorm(h, axis=-1), L0_attn_Wqkv, L0_attn_Wproj, L0_attn_bproj, L0_attn_ln_g, L0_attn_ln_b, L0_attn_Wg1, L0_attn_bg1, L0_attn_Wg2, L0_attn_bg2)
    h = h + _L0_ffn_ref(_layernorm(h, axis=-1), L0_ffn_attention_mask, L0_ffn_wr, L0_ffn_br, L0_ffn_w1, L0_ffn_b1, L0_ffn_w2, L0_ffn_b2)
    return h


_drawn_inputs = setup_inputs


def setup_inputs(seed=0):
    import zlib

    import numpy as np

    out = dict(_drawn_inputs(seed))
    spreads = {'L0_tok_b_o1': (0.0, 0.1),
     'L0_tok_ln_g': (1.0, 0.2),
     'L0_tok_ln_b': (0.0, 0.1),
     'L0_tok_b_o2': (0.0, 0.1),
     'L0_attn_bproj': (0.0, 0.1),
     'L0_attn_ln_g': (1.0, 0.6),
     'L0_attn_ln_b': (0.0, 0.8),
     'L0_attn_bg1': (0.0, 0.8),
     'L0_attn_bg2': (0.0, 0.8),
     'L0_ffn_b1': (0.0, 0.8),
     'L0_ffn_b2': (0.0, 0.512)}
    factors = {'L0_attn_Wqkv': 3.841,
     'L0_attn_Wproj': 3.853,
     'L0_attn_Wg1': 8.0,
     'L0_attn_Wg2': 8.0,
     'L0_ffn_wr': 2.787,
     'L0_ffn_w1': 3.23,
     'L0_ffn_w2': 2.995}
    for name, (base, spread) in spreads.items():
        noise = np.random.default_rng([zlib.crc32(name.encode()), seed]).standard_normal(out[name].shape)
        drawn = base * np.exp(spread * noise) if base else spread * noise
        out[name] = jnp.asarray(drawn.astype(out[name].dtype))
    for name, factor in factors.items():
        out[name] = (out[name] * factor).astype(out[name].dtype)
    return out
```

```python
from contextlib import ExitStack

import concourse.bass as bass
from concourse import mybir

F32 = mybir.dt.float32
BF16 = mybir.dt.bfloat16
I32 = mybir.dt.int32
U32 = mybir.dt.uint32
ALU = mybir.AluOpType
ACT = mybir.ActivationFunctionType
AX = mybir.AxisListType

P = 128
B, C, H, W = 16, 256, 128, 128
PX = H * W
CH = C // P
DS = 4
NQ = (H // DS) * (W // DS)
NT = NQ // P
NH = 8
DH = C // NH
GQ = P // NH
NG = NQ // GQ
GT = P // GQ
HG = 4
NHALF = NG // HG
RING = 4
HQ = HG * GQ
FO = C // DS
HID = 4 * C
KK = NQ // 2 - 1
OFFSET_SCALE = 4.0
EPS = 1e-5
SCALE = float(DH) ** -0.5
CR = 4
CPX = CR * W
NPAIR = H // CR // 2
TPAIRS = NPAIR // 2
TC = 512
NC2 = NQ // TC
SLOTS = 4
FAR = -1.0e30

CONST_COLS = {}
_at = 0
for _name, _n in (("ident", P), ("own16", P), ("group8", GT), ("head4", 4), ("lower", P), ("upper", P), ("heads", P),
                  ("refs", 2 * NG), ("qweight", NT * 4), ("qindex", NT * 2), ("same_q", P), ("far_q", P)):
    CONST_COLS[_name] = (_at, _at + _n)
    _at += _n
NCONST = _at

END_ORDER = ("norm1", "T", "xaT", "qin", "T", "qfT", "norm2", "qproj", "T", "xnT", "T", "qkv", "qhidden", "T", "ek",
             "qoff", "hgate", "ctx", "T", "qpoints", "gate", "mix", "T", "proj", "norm3", "xfT", "rank", "T", "ffn", "store")
Q_STAGES = ("qin", "qfT", "qproj", "qhidden", "qoff", "qpoints")


def build_tower(nc, x, consts, wq_t, wk, wv_t, wo1, bo1, og, ob, wo2, bo2, wqkv, wproj, bproj, ag, ab, wg1, bg1, wg2, bg2,
                wr, br, w1, b1, w2, b2, out):
    with ExitStack() as ctx:
        def sb(name, shape, dt=F32):
            return ctx.enter_context(nc.sbuf_tensor(name, shape, dt))

        def sem(name):
            return ctx.enter_context(nc.semaphore(name))

        scratch = nc.dram_tensor("pixel_rows", [SLOTS * PX, C], F32, kind="Internal").ap()
        pixel_pairs = scratch.rearrange("(a b) c -> a b c", b=2)

        K_ = sb("consts", [P, NCONST])

        def const(name):
            a, e = CONST_COLS[name]
            return K_[:, a:e]

        ident = const("ident")
        WQ = sb("WQ", [P, CH, C])
        WKP = sb("WKP", [P, NH, C])
        WV = sb("WV", [P, CH, C])
        WO1 = sb("WO1", [P, CH, FO])
        WO2 = sb("WO2", [FO, 2 * NH])
        WQKV = sb("WQKV", [P, CH, 3 * C])
        WP = sb("WP", [P, CH, C])
        WG1 = sb("WG1", [P, CH, FO])
        WG2 = sb("WG2", [FO, C])
        W1 = sb("W1", [P, CH, HID])
        W2 = sb("W2", [P, HID // P, C])
        rows = sb("rows", [P, 3 * FO + 2 * NH + 3 * C + 1])
        o = 0
        BO1, o = rows[:, o:o + FO], o + FO
        OG, o = rows[:, o:o + FO], o + FO
        OB, o = rows[:, o:o + FO], o + FO
        BO2, o = rows[:, o:o + 2 * NH], o + 2 * NH
        BPROJ, o = rows[:, o:o + C], o + C
        WR, o = rows[:, o:o + C], o + C
        B2, o = rows[:, o:o + C], o + C
        BR, o = rows[:, o:o + 1], o + 1
        cols = sb("cols", [P, 2 + 2 + 1 + 2 + HID // P])
        AG, AB, BG1, BG2, B1 = cols[:, 0:2], cols[:, 2:4], cols[0:FO, 4:5], cols[:, 5:7], cols[:, 7:7 + HID // P]
        same_q = sb("same_q", [P, P], BF16)
        far_q = sb("far_q", [P, P], BF16)

        xin = [sb(f"xin{i}", [P, CH, CPX]) for i in range(2)]
        xrow = [sb(f"xrow{i}", [P, CR, C]) for i in range(2)]
        xg = sb("xg", [P, GT, 2, 2 * C])
        smp = sb("smp", [P, RING, HG, C])
        smpT = sb("smpT", [P, 2, HG, CH, P])
        qkT = sb("qkT", [P, 2, CH, HQ, NH])
        probs = sb("probs", [P, 2, 2, HG, P])
        accT = sb("accT", [P, CH, P, NH])
        queT = sb("queT", [P, CH, NQ])
        hbuf = sb("hbuf", [P, NT, C])
        big = sb("big", [P, 4, NT * C])
        hg = sb("hg", [FO, NQ])
        xa = big[:, 0, :].rearrange("p (t c) -> p t c", t=NT)
        ekT = big[:, 0, :].rearrange("p (h n) -> p h n", h=CH)
        xaT = big[:, 1, :].rearrange("p (h n) -> p h n", h=CH)
        xnT = big[:, 2, :].rearrange("p (h n) -> p h n", h=CH)
        qT = big[:, 3, :].rearrange("p (h n) -> p h n", h=CH)
        hid = big[:, 2:4, :].rearrange("p a (k n) -> p (a k) n", n=TC)
        smpT_flat = smpT[:].rearrange("p a g h n -> p (a g h n)")
        vtok = smpT_flat.rearrange("p (t c) -> p t c", t=NT)
        ektok = probs[:].rearrange("p a b g n -> p (a b g n)").rearrange("p (t c) -> p t c", t=NT)
        wrow = smpT_flat[:, 0:NQ]
        ytmp = smpT_flat[:, NQ:NQ + 2 * 2 * C].rearrange("p (i t c) -> p i t c", i=2, t=2)
        smp_flat = smp[:].rearrange("p a g c -> p (a g c)")
        sq = smp_flat[:, 0:NT * C].rearrange("p (t c) -> p t c", t=NT)
        qhT = smp_flat[0:FO, NT * C:NT * C + NQ]
        qo = smp_flat[:, NT * C + NQ:NT * C + NQ + NT * FO].rearrange("p (t f) -> p t f", t=NT)
        qo2 = smp_flat[:, NT * C + NQ + NT * FO:NT * C + NQ + 2 * NT * FO].rearrange("p (t f) -> p t f", t=NT)
        qfT = accT[:].rearrange("p h q n -> p h (q n)")
        spread = qkT[:].rearrange("p a h q n -> p a (h q n)").rearrange("p a (t n) -> p a t n", t=NT)

        stats = sb("stats", [P, NT, 6])
        mv = sb("mv", [P, NT, 2])
        var = sb("var", [P, NT])
        std = sb("std", [P, NT])
        qsum = sb("qsum", [P, 4, NT])
        qoff = sb("qoff", [P, NT, NH, 2])
        pos = sb("pos", [P, 2, NG])
        posi = sb("posi", [P, 2, NG], I32)
        posf = sb("posf", [P, 2, NG])
        gtf = sb("gtf", [P, 2, NG])
        frac = sb("frac", [P, 2, 2, NG])
        idxf = sb("idxf", [P, NG])
        base = sb("base", [P, 1])
        wrap = sb("wrap", [P, 1])
        wgt = sb("wgt", [P, 4, NG])
        idx_all = sb("idx_all", [P, NG, 2], U32)
        idx_now = [sb(f"idx_now{i}", [P, GT, 2], U32) for i in range(2)]
        qidx = sb("qidx", [P, NT, 2], U32)
        smax = sb("smax", [P, 2, HG])
        nmax = sb("nmax", [P, 2, HG])
        ssum = sb("ssum", [P, 2, HG])
        srec = sb("srec", [P, 2, HG])
        kmax = sb("kmax", [P, CH, NC2])
        knmax = sb("knmax", [P, CH])
        ksum = sb("ksum", [P, CH, NC2])
        krec = sb("krec", [P, CH])
        ctxm = sb("ctxm", [P, CH, P])
        wtok = sb("wtok", [P, NT])
        wsel = sb("wsel", [P, NT])
        cnt = sb("cnt", [P, 4, NT])
        rnk = sb("rnk", [P, NT])
        junk = sb("junk", [P, NQ], BF16)

        bank = [ctx.enter_context(nc.psum_tensor(f"bank{i}", [P, TC], F32)) for i in range(8)]
        rows_bank = bank[0:2]
        smpT_bank = bank[2:4]
        score_bank, probT_bank = bank[4], bank[5]
        work_bank = bank[6:8]
        end_banks = bank[2:8]

        loaded = sem("weights_loaded")
        ready0 = sem("weights_ready")
        x_loaded = [sem(f"x_loaded{i}") for i in range(2)]
        rows_turned = sem("rows_turned")
        rows_act = sem("rows_copied_by_act")
        rows_dve = sem("rows_copied_by_dve")
        rows_stored = [sem(f"rows_stored{i}") for i in range(2)]
        gathered = [sem(f"gathered{i}") for i in range(GT)]
        first_term = sem("first_term")
        sampled = sem("sampled")
        qidx_ready = sem("query_index_ready")
        points_ready = sem("points_ready")
        idx_copied = sem("index_copied")
        qk_done, qk_copied = sem("qk_done"), sem("qk_copied")
        smpT_done, smpT_copied = sem("smpT_done"), sem("smpT_copied")
        scores_done, max_ready, exp_done = sem("scores_done"), sem("max_ready"), sem("exp_done")
        probs_ready, probT_done, probT_copied = sem("probs_ready"), sem("probT_done"), sem("probT_copied")
        acc_done, acc_copied = sem("acc_done"), sem("acc_copied")
        tok_done, tok_copied = sem("tok_done"), sem("tok_copied")
        var_ready, std_ready = sem("var_ready"), sem("std_ready")
        qvar_ready, qstd_ready = sem("qvar_ready"), sem("qstd_ready")
        xa_ready, xaT_done, xaT_copied = sem("xa_ready"), sem("xaT_done"), sem("xaT_copied")
        xn_ready, xnT_done, xnT_copied = sem("xn_ready"), sem("xnT_done"), sem("xnT_copied")
        qfT_done, qfT_copied = sem("qfT_done"), sem("qfT_copied")
        queT_done, queT_copied = sem("queT_done"), sem("queT_copied")
        o1_done, o1_copied = sem("o1_done"), sem("o1_copied")
        qh_normed, qh_ready, qhT_done, qhT_copied = sem("qh_normed"), sem("qh_ready"), sem("qhT_done"), sem("qhT_copied")
        off_done, off_copied, spread_ready, pts_done, pts_copied = (
            sem("off_done"), sem("off_copied"), sem("spread_ready"), sem("pts_done"), sem("pts_copied"))
        v_done, v_copied, q_done, q_copied = sem("v_done"), sem("v_copied"), sem("q_done"), sem("q_copied")
        k_done, kmax_ready, k_exped = sem("k_done"), sem("kmax_ready"), sem("k_exped")
        ek_done, ek_copied, ctx_done, ctx_copied = sem("ek_done"), sem("ek_copied"), sem("ctx_done"), sem("ctx_copied")
        hg_done, hg_copied, gate_done, gate_copied = sem("hg_done"), sem("hg_copied"), sem("gate_done"), sem("gate_copied")
        mix_done, mix_copied, proj_done, proj_copied = sem("mix_done"), sem("mix_copied"), sem("proj_done"), sem("proj_copied")
        xf_ready, xfT_done, xfT_copied = sem("xf_ready"), sem("xfT_done"), sem("xfT_copied")
        w_ready, wrow_done, wrow_copied = sem("w_ready"), sem("wrow_done"), sem("wrow_copied")
        hid_done, hid_copied, y_done, y_copied = sem("hid_done"), sem("hid_copied"), sem("y_done"), sem("y_copied")
        out_stored = sem("out_stored")
        slots_taken = sem("slots_taken")
        filled = sem("scratch_filled")
        dve_step = sem("dve_step")
        act_step = sem("act_step")

        def end_stages(attend, query, turn):
            return [s for s in END_ORDER if (turn if s == "T" else query if s in Q_STAGES else attend)]

        def images(engine, sample, finish):
            finish(-1, attend=False, query=True, turn=True)
            with engine.Fori(0, B - 2) as b:
                sample(b, turn=True)
                finish(b, attend=True, query=True, turn=True)
            sample(B - 2, turn=True)
            finish(B - 2, attend=True, query=True, turn=False)
            sample(B - 1, turn=False)
            finish(B - 1, attend=True, query=False, turn=False)

        def quads(engine, quad):
            quad(0, first=True, last=False)
            with engine.Fori(1, NHALF // RING - 1) as u:
                quad(u, first=False, last=False)
            quad(NHALF // RING - 1, first=False, last=True)

        class Chain:

            def __init__(self, engine, s):
                self.engine, self.sem, self.n = engine, s, 0

            def step(self, ins):
                ins.then_inc(self.sem, 1)
                self.n += 1
                return self.n

            def wait(self, n=None):
                self.engine.wait_ge(self.sem, self.n if n is None else n)

            def link(self, ins):
                self.step(ins)
                self.wait()

            def clear(self):
                if self.n:
                    self.wait()
                    self.engine.sem_clear(self.sem)
                    self.n = 0

        def bank_map(stages):
            takes = {"xaT": [("xaT", 4)], "xnT": [("xnT", 4)], "xfT": [("xfT", 4)], "qfT": [("qfT", 4)],
                     "qproj": [("o1", 1), ("queT", 4)], "qkv": [("k", 4), ("v", 4), ("q", 4)], "qhidden": [("qhT", 2)],
                     "ek": [("ek", 4)], "qoff": [("off", 1)], "hgate": [("hg", 2)], "ctx": [("ctx", 1)], "qpoints": [("pts", 1)],
                     "gate": [("gate", 4)], "mix": [("mix", 4)], "proj": [("proj", 4)], "rank": [("wrow", 2)],
                     "ffn": [("hid", 8), ("y", 2), ("hid", 8), ("y", 2)]}
            at, where = 0, {}
            for s in stages:
                for name, n in takes.get(s, ()):
                    for _ in range(n):
                        where.setdefault(name, []).append(at % len(end_banks))
                        at += 1
            return lambda name, i: end_banks[where[name][i]][:]

        block = ctx.enter_context(nc.Block())

        @block.sync
        def _(sp):
            def halves(a, n):
                return a.rearrange("(k p) n -> p k n", p=P) if n else a

            for dst, src in ((K_[:], consts), (WQ[:], halves(wq_t, 1)), (qkT[:].rearrange("p a h q n -> p a (h q n)")[:, :, 0:C],
                             halves(wk, 1)), (WV[:], halves(wv_t, 1)), (WO1[:], halves(wo1, 1)), (WO2[:], wo2),
                             (WQKV[:], halves(wqkv, 1)), (WP[:], halves(wproj, 1)), (WG1[:], halves(wg1, 1)), (WG2[:], wg2),
                             (W1[:], halves(w1, 1)), (W2[:], halves(w2, 1))):
                sp.dma_start(dst, src).then_inc(loaded, 16)
            for dst, src, n in ((BO1, bo1, FO), (OG, og, FO), (OB, ob, FO), (BO2, bo2, 2 * NH), (BPROJ, bproj, C), (WR, wr, C),
                                (B2, b2, C), (BR, br, 1)):
                sp.dma_start(dst, src.rearrange("(o n) -> o n", o=1).broadcast_to([P, n])).then_inc(loaded, 16)
            for dst, src, p in ((AG, ag, P), (AB, ab, P), (BG1, bg1, FO), (BG2, bg2, P), (B1, b1, P)):
                sp.dma_start(dst, src.rearrange("(k p) -> p k", p=p), allow_slow_non_contiguous=True).then_inc(loaded, 16)

            def turn_pair(image, jj, free=True):
                pair = image * NPAIR + jj
                for i in range(2):
                    if free:
                        sp.wait_ge(rows_turned, pair * 4 + 2 * i - 2)
                    src = x[image, :, :, :].rearrange("(h p) r w -> p h (r w)", h=CH)
                    sp.dma_start(xin[i][:], src[:, :, bass.ds((jj * 2 + i) * CPX, CPX)]).then_inc(x_loaded[i], 16)
                for i in range(2):
                    sp.wait_ge(rows_act, pair * 2 + i + 1)
                    sp.wait_ge(rows_dve, pair * 2 + i + 1)
                    dst = scratch[bass.ds(image % SLOTS * PX + (jj * 2 + i) * CPX, CPX), :].rearrange("(r p) c -> p r c", p=P)
                    sp.dma_start(dst, xrow[i][:]).then_inc(rows_stored[i], 16)

            sp.wait_ge(ready0, 1)
            fill_rows = P * GT * 2 * 2
            with nc.sync.Fori(0, SLOTS * PX // fill_rows) as i:
                dst = scratch[bass.ds(i * fill_rows, fill_rows), :].rearrange("(p a) c -> p (a c)", p=P)
                sp.dma_start(dst, xg[:].rearrange("p s r n -> p (s r n)")).then_inc(filled, 16)
            sp.wait_ge(filled, 16 * (SLOTS * PX // fill_rows))

            turn_pair(0, 0, free=False)
            with nc.sync.Fori(1, NPAIR) as jj:
                turn_pair(0, jj)

            def sample(b, turn):
                if turn:
                    with nc.sync.Fori(TPAIRS, NPAIR) as jj:
                        turn_pair(b + 1, jj)

            def finish(b, attend, query, turn):
                n = 0
                for s in end_stages(attend, query, turn):
                    if s == "T":
                        turn_pair(b + 2, n)
                        n += 1
                    if s == "store":
                        sp.wait_ge(y_copied, (b + 1) * NT)
                        dst = out[bass.ds(b * NQ, NQ), :].rearrange("(t p) c -> p t c", p=P)
                        sp.dma_start(dst, hbuf[:]).then_inc(out_stored, 16)

            images(nc.sync, sample, finish)
            sp.wait_ge(out_stored, 16 * B)
            for i in range(2):
                sp.wait_ge(rows_stored[i], 16 * NPAIR * B)

        @block.gpsimd
        def _(pool):
            def free_slot(group):
                pool.wait_ge(sampled, group + 1)
                pool.sem_inc(slots_taken, 1)

            def gather(slot, r, index):
                nc.gpsimd.indirect_dma_start(out=xg[:, slot, r, :], out_offset=None, in_=pixel_pairs,
                                             in_offset=bass.IndirectOffsetOnAxis(ap=index, axis=1)).then_inc(gathered[slot], 16)

            def sample(b, turn):
                with nc.gpsimd.Fori(0, NT // 2) as v:
                    for i in range(2):
                        t = v * 2 + i
                        for slot in range(GT):
                            pool.wait_ge(gathered[slot], (b * (NT + 1) + t) * 32)
                        pool.wait_ge(points_ready, b + 1)
                        nc.gpsimd.tensor_copy(idx_now[i][:], idx_all[:, bass.ds(t * GT, GT), :]).then_inc(idx_copied, 1)
                        pool.wait_ge(idx_copied, b * NT + t + 1)
                        for g in range(GT):
                            free_slot(b * (NT + NG) + NT + t * GT + g)
                            for r in range(2):
                                gather(g, r, idx_now[i][:, g, r:r + 1])

            def finish(b, attend, query, turn):
                if not query:
                    return
                c = b + 1
                for i in range(2):
                    pool.wait_ge(rows_stored[i], (c + 1) * (16 * NPAIR))
                pool.wait_ge(qidx_ready, c + 1)
                for g in range(NT):
                    free_slot(c * (NT + NG) + g)
                    for r in range(2):
                        gather(g, r, qidx[:, g, r:r + 1])

            images(nc.gpsimd, sample, finish)

        @block.tensor
        def _(pe):
            mm, tr = nc.tensor.matmul, nc.tensor.transpose
            pe.wait_ge(ready0, 1)

            def turn_pair(image, jj):
                pair = image * NPAIR + jj
                for i in range(2):
                    turn_chunk(pair, i)

            def turn_chunk(pair, i):
                pe.wait_ge(x_loaded[i], pair * 16 + 16)
                for r in range(2):
                    pe.wait_ge((rows_act, rows_dve)[r], pair * 2 + i)
                    for rr in range(2):
                        for h in range(CH):
                            row = 2 * r + rr
                            last = tr(rows_bank[r][:, (rr * CH + h) * P:(rr * CH + h + 1) * P],
                                      xin[i][:, h, row * W:(row + 1) * W], ident)
                    last.then_inc(rows_turned, 1)

            with nc.tensor.Fori(0, NPAIR) as jj:
                turn_pair(0, jj)

            def sample(b, turn):
                def qk(k, kap, u):
                    if not isinstance(k, int) or k >= 2:
                        pe.wait_ge(acc_copied, b * (2 * NHALF) + k * 2 - 2)
                    if kap % 2 == 1:
                        pe.wait_ge(tok_copied, b * NT + u * 2 + kap // 2)
                    for h in range(CH):
                        for n in range(NH):
                            last = mm(work_bank[h][:, n * HQ:(n + 1) * HQ], WKP[:, n, h * P:(h + 1) * P],
                                      queT[:, n * DH // P, bass.ds(k * HQ, HQ)], start=True, stop=True)
                        last.then_inc(qk_done, 1)

                def turn_samples(k, kap):
                    for pr in range(2):
                        pe.wait_ge(sampled, b * (NT + NG) + GT + NT + k * HG + 2 * pr + 2)
                        if not isinstance(k, int) or k >= 1:
                            pe.wait_ge(smpT_copied, b * (2 * NHALF) + k * 2 + pr - 1)
                        for g in range(2):
                            for h in range(CH):
                                last = tr(smpT_bank[pr][:, (g * CH + h) * P:(g * CH + h + 1) * P],
                                          smp[:, kap, 2 * pr + g, h * P:(h + 1) * P], ident)
                        last.then_inc(smpT_done, 1)

                def turn_probs(k, kap):
                    pe.wait_ge(probs_ready, b * NHALF + k + 1)
                    for g in range(HG):
                        last = tr(probT_bank[:, g * P:(g + 1) * P], probs[:, 0, kap % 2, g, :], ident)
                    last.then_inc(probT_done, 1)

                def scores(k, kap):
                    hf = kap % 2
                    pe.wait_ge(smpT_copied, b * (2 * NHALF) + k * 2 + 2)
                    pe.wait_ge(qk_copied, b * (2 * NHALF) + k * 2 + 2)
                    pe.wait_ge(exp_done, b * NHALF + k)
                    for g in range(HG):
                        o_ = score_bank[:, g * P:(g + 1) * P]
                        mm(o_, same_q[:], far_q[:], start=True, stop=False)
                        for h in range(CH):
                            last = mm(o_, qkT[:, hf, h, g * GQ:(g + 1) * GQ, :], smpT[:, hf, g, h, :], start=False, stop=h == CH - 1)
                    last.then_inc(scores_done, 1)

                def weigh(k, kap):
                    pe.wait_ge(probT_copied, b * NHALF + k + 1)
                    for pr in range(2):
                        for g in range(2):
                            for h in range(CH):
                                last = mm(work_bank[pr][:, (g * CH + h) * P:(g * CH + h + 1) * P],
                                          smp[:, kap, 2 * pr + g, h * P:(h + 1) * P], probs[:, 1, kap % 2, 2 * pr + g, :],
                                          start=True, stop=True)
                        last.then_inc(acc_done, 1)

                def tokens(t):
                    pe.wait_ge(acc_copied, b * (2 * NHALF) + t * 4 + 4)
                    for n in range(NH):
                        for h in range(CH):
                            last = mm(work_bank[0][:, n * DH:(n + 1) * DH], accT[:, h, :, n], WV[:, h, n * DH:(n + 1) * DH],
                                      start=h == 0, stop=h == CH - 1)
                    last.then_inc(tok_done, 1)

                def quad(u, first, last):
                    for kap in range(RING):
                        k = u * RING + kap
                        have = not (first and kap == 0)
                        qk(k, kap, u)
                        turn_samples(k, kap)
                        if have:
                            turn_probs(k - 1, (kap - 1) % RING)
                        scores(k, kap)
                        if have:
                            weigh(k - 1, (kap - 1) % RING)
                        if turn:
                            turn_chunk((b + 1) * NPAIR + TPAIRS + u * 2 + kap // 2, kap % 2)
                        if have and kap % 2 == 0:
                            tokens(u * 2 + kap // 2 - 1)

                quads(nc.tensor, quad)
                turn_probs(NHALF - 1, RING - 1)
                pe.wait_ge(acc_copied, b * (2 * NHALF) + 2 * NHALF - 2)
                weigh(NHALF - 1, RING - 1)
                tokens(NT - 1)

            class Ring:

                def __init__(self):
                    self.at, self.freed = 0, [None] * len(end_banks)

                def take(self, copied, value):
                    i = self.at % len(end_banks)
                    if self.freed[i]:
                        pe.wait_ge(*self.freed[i])
                    self.at, self.freed[i] = self.at + 1, (copied, value)
                    return end_banks[i]

                def copied(self, s, value):
                    pe.wait_ge(s, value)
                    self.freed = [None if f and f[0] is s else f for f in self.freed]

                def drain(self):
                    n = len(end_banks)
                    for i in range(self.at + n - 1, self.at - 1, -1):
                        if self.freed[i % n]:
                            self.copied(*self.freed[i % n])

            def finish(b, attend, query, turn):
                ring = Ring()
                c = b + 1

                def turn_tokens(src, ready, per, done, copied, im):
                    for h in range(CH):
                        for c2 in range(NC2):
                            if h == 0:
                                pe.wait_ge(ready, im * per + (c2 + 1) * per // NC2)
                            bk = ring.take(copied, im * 4 + h * NC2 + c2 + 1)
                            for t in range(4):
                                last = tr(bk[:, t * P:(t + 1) * P], src[:, c2 * 4 + t, h * P:(h + 1) * P], ident)
                            last.then_inc(done, 1)

                def project(wt, col, src, done, copied, im, m=P):
                    for j, cc in enumerate(col):
                        for c2 in range(NC2):
                            bk = ring.take(copied, im * len(col) * NC2 + j * NC2 + c2 + 1)
                            for h in range(CH):
                                last = mm(bk[0:m, :], wt[:, h, cc:cc + m], src[:, h, c2 * TC:(c2 + 1) * TC],
                                          start=h == 0, stop=h == CH - 1)
                            last.then_inc(done, 1)

                def s_xaT():
                    pe.wait_ge(tok_copied, (b + 1) * NT)
                    turn_tokens(xa, xa_ready, NT, xaT_done, xaT_copied, b)

                def s_xnT():
                    turn_tokens(xa, xn_ready, NT, xnT_done, xnT_copied, b)

                def s_xfT():
                    turn_tokens(xa, xf_ready, NT, xfT_done, xfT_copied, b)

                def s_qfT():
                    for h in range(CH):
                        for c2 in range(NC2):
                            if h == 0:
                                pe.wait_ge(sampled, c * (NT + NG) + GT + (c2 + 1) * 4)
                            bk = ring.take(qfT_copied, c * 4 + h * NC2 + c2 + 1)
                            for t in range(4):
                                last = tr(bk[:, t * P:(t + 1) * P], sq[:, c2 * 4 + t, h * P:(h + 1) * P], ident)
                            last.then_inc(qfT_done, 1)

                def s_qproj():
                    ring.copied(qfT_copied, c * 4 + 4)
                    bk = ring.take(o1_copied, c + 1)
                    for t in range(NT):
                        for h in range(CH):
                            last = mm(bk[:, t * FO:(t + 1) * FO], qfT[:, h, t * P:(t + 1) * P], WO1[:, h, :], start=h == 0, stop=h == CH - 1)
                    last.then_inc(o1_done, 1)
                    project(WQ, (0, P), qfT, queT_done, queT_copied, c)

                def s_qkv():
                    ring.copied(xaT_copied, b * 4 + 4)
                    project(WQKV, (C, C + P), xaT, k_done, k_exped, b)
                    for v in range(NT // 2):
                        bk = ring.take(v_copied, b * 4 + v + 1)
                        for i in range(2):
                            for h in range(CH):
                                last = mm(bk[:, i * C:(i + 1) * C], xaT[:, h, (2 * v + i) * P:(2 * v + i + 1) * P],
                                          WQKV[:, h, 2 * C:3 * C], start=h == 0, stop=h == CH - 1)
                        last.then_inc(v_done, 1)
                    project(WQKV, (0, P), xaT, q_done, q_copied, b)

                def s_qhidden():
                    for c2 in range(NC2):
                        pe.wait_ge(ready0, 1)
                        pe.wait_ge(qh_ready, c + 1)
                        bk = ring.take(qhT_copied, c * 2 + c2 + 1)
                        for t in range(4):
                            last = tr(bk[0:FO, t * P:(t + 1) * P], qo2[:, c2 * 4 + t, :], ident)
                        last.then_inc(qhT_done, 1)

                def s_ek():
                    ring.copied(k_exped, b * 4 + 4)
                    for v in range(NT // 2):
                        bk = ring.take(ek_copied, b * 4 + v + 1)
                        for i in range(2):
                            for h in range(CH):
                                last = tr(bk[:, (i * CH + h) * P:(i * CH + h + 1) * P], ekT[:, h, (2 * v + i) * P:(2 * v + i + 1) * P], ident)
                        last.then_inc(ek_done, 1)

                def s_qoff():
                    ring.copied(qhT_copied, c * 2 + 2)
                    bk = ring.take(off_copied, c + 1)
                    for t in range(NT):
                        last = mm(bk[:, t * 2 * NH:(t + 1) * 2 * NH], qhT[:, t * P:(t + 1) * P], WO2[:], start=True, stop=True)
                    last.then_inc(off_done, 1)

                def s_hgate():
                    ring.copied(xnT_copied, b * 4 + 4)
                    project(WG1, (0,), xnT, hg_done, hg_copied, b, m=FO)

                def s_ctx():
                    ring.copied(v_copied, b * 4 + 4)
                    ring.copied(ek_copied, b * 4 + 4)
                    bk = ring.take(ctx_copied, b + 1)
                    for h in range(CH):
                        for t in range(NT):
                            last = mm(bk[:, h * P:(h + 1) * P], ektok[:, t, h * P:(h + 1) * P], vtok[:, t, h * P:(h + 1) * P],
                                      start=t == 0, stop=t == NT - 1)
                    last.then_inc(ctx_done, 1)

                def s_qpoints():
                    pe.wait_ge(spread_ready, c + 1)
                    bk = ring.take(pts_copied, c + 1)
                    for a in range(2):
                        for t in range(NT):
                            last = mm(bk[:, a * NG + t * GT:a * NG + (t + 1) * GT], spread[:, a, t, :], const("group8"), start=True, stop=True)
                    last.then_inc(pts_done, 1)

                def s_gate():
                    ring.copied(hg_copied, b * 2 + 2)
                    for h in range(CH):
                        for c2 in range(NC2):
                            bk = ring.take(gate_copied, b * 4 + h * NC2 + c2 + 1)
                            mm(bk[:], WG2[:, h * P:(h + 1) * P], hg[:, c2 * TC:(c2 + 1) * TC], start=True, stop=True).then_inc(gate_done, 1)

                def s_mix():
                    ring.copied(ctx_copied, b + 1)
                    ring.copied(q_copied, b * 4 + 4)
                    for h in range(CH):
                        for c2 in range(NC2):
                            bk = ring.take(mix_copied, b * 4 + h * NC2 + c2 + 1)
                            mm(bk[:], ctxm[:, h, :], qT[:, h, c2 * TC:(c2 + 1) * TC], start=True, stop=True).then_inc(mix_done, 1)

                def s_proj():
                    ring.copied(mix_copied, b * 4 + 4)
                    for v in range(NT // 2):
                        bk = ring.take(proj_copied, b * 4 + v + 1)
                        for i in range(2):
                            for h in range(CH):
                                last = mm(bk[:, i * C:(i + 1) * C], xaT[:, h, (2 * v + i) * P:(2 * v + i + 1) * P], WP[:, h, :],
                                          start=h == 0, stop=h == CH - 1)
                        last.then_inc(proj_done, 1)

                def s_rank():
                    pe.wait_ge(w_ready, b + 1)
                    for c2 in range(NC2):
                        bk = ring.take(wrow_copied, b * 2 + c2 + 1)
                        for t in range(4):
                            tt = c2 * 4 + t
                            last = tr(bk[:, t * P:(t + 1) * P], wtok[:, tt:tt + 1].broadcast_to([P, P]), ident)
                        last.then_inc(wrow_done, 1)

                def s_ffn():
                    ring.copied(xfT_copied, b * 4 + 4)
                    for c2 in range(NC2):
                        if c2:
                            ring.copied(hid_copied, b * 16 + c2 * 8)
                        for j in range(HID // P):
                            bk = ring.take(hid_copied, b * 16 + c2 * 8 + j + 1)
                            for h in range(CH):
                                last = mm(bk[:], W1[:, h, j * P:(j + 1) * P], xaT[:, h, c2 * TC:(c2 + 1) * TC], start=h == 0, stop=h == CH - 1)
                            last.then_inc(hid_done, 1)
                        ring.copied(hid_copied, b * 16 + c2 * 8 + 8)
                        for v in range(2):
                            bk = ring.take(y_copied, b * NT + c2 * 4 + 2 * v + 2)
                            for i in range(2):
                                for j in range(HID // P):
                                    last = mm(bk[:, i * C:(i + 1) * C], hid[:, j, (2 * v + i) * P:(2 * v + i + 1) * P], W2[:, j, :],
                                              start=j == 0, stop=j == HID // P - 1)
                            last.then_inc(y_done, 1)

                run = {"xaT": s_xaT, "xnT": s_xnT, "xfT": s_xfT, "qfT": s_qfT, "qproj": s_qproj, "qkv": s_qkv, "qhidden": s_qhidden,
                       "ek": s_ek, "qoff": s_qoff, "hgate": s_hgate, "ctx": s_ctx, "qpoints": s_qpoints, "gate": s_gate,
                       "mix": s_mix, "proj": s_proj, "rank": s_rank, "ffn": s_ffn}
                n = 0
                for s in end_stages(attend, query, turn):
                    if s == "T":
                        turn_pair(b + 2, n)
                        n += 1
                    elif s in run:
                        run[s]()
                ring.drain()

            images(nc.tensor, sample, finish)

        @block.scalar
        def _(act):
            def fn(o_, i_, f, **kw):
                return nc.scalar.activation(o_, i_, f, **kw)

            act.wait_ge(ready0, 1)

            def turn_chunk(pair, i):
                pe_n = pair * 4 + 2 * i + 1
                act.wait_ge(rows_turned, pe_n)
                act.wait_ge(rows_stored[i], pair * 16)
                fn(xrow[i][:, 0:2, :], rows_bank[0][:], ACT.Copy).then_inc(rows_act, 1)

            def turn_pair(image, jj):
                for i in range(2):
                    turn_chunk(image * NPAIR + jj, i)

            with nc.scalar.Fori(0, NPAIR) as jj:
                turn_pair(0, jj)

            def sample(b, turn):
                def first_terms(k, kap):
                    if not isinstance(k, int) or k >= RING:
                        act.wait_ge(acc_done, b * (2 * NHALF) + k * 2 + 2 - 2 * RING)
                    for g in range(HG):
                        slot = (kap * HG + g) % GT
                        act.wait_ge(gathered[slot], (b * (NT + 1) + 2 + state["u"] * 2 + (kap // 2)) * 32)
                        fn(smp[:, kap % RING, g, :], xg[:, slot, 0, 0:C], ACT.Copy,
                           scale=wgt[:, 0, bass.ds(k * HG + g, 1)]).then_inc(first_term, 1)

                state = {}

                def copy_samples(k, kap):
                    if not isinstance(k, int) or k >= 2:
                        act.wait_ge(scores_done, b * NHALF + k - 1)
                    for pr in range(2):
                        act.wait_ge(smpT_done, b * (2 * NHALF) + k * 2 + pr + 1)
                        fn(smpT[:, kap % 2, 2 * pr:2 * pr + 2, :, :].rearrange("p g h n -> p (g h n)"), smpT_bank[pr][:], ACT.Copy)\
                            .then_inc(smpT_copied, 1)

                def exps(k, kap):
                    hf = kap % 2
                    act.wait_ge(max_ready, b * NHALF + k + 1)
                    if not isinstance(k, int) or k >= 2:
                        act.wait_ge(probT_done, b * NHALF + k - 1)
                    for g in range(HG):
                        last = fn(probs[:, 0, hf, g, :], score_bank[:, g * P:(g + 1) * P], ACT.Exp, bias=nmax[:, hf, g:g + 1],
                                  scale=SCALE, accum_out=ssum[:, hf, g:g + 1])
                    last.then_inc(exp_done, 1)

                def copy_acc(k, kap):
                    if kap % 2 == 0:
                        act.wait_ge(tok_done, b * NT + tile_of(k))
                    for pr in range(2):
                        q0 = (kap % 2) * HQ + pr * 2 * GQ
                        act.wait_ge(acc_done, b * (2 * NHALF) + k * 2 + pr + 1)
                        for h in range(CH):
                            src = work_bank[pr][:].rearrange("p (g h q n) -> p h g (q n)", g=2, h=CH, n=NH)[:, h]
                            last = fn(accT[:, h, q0:q0 + 2 * GQ, :].rearrange("p (g q) n -> p g (q n)", g=2), src, ACT.Copy)
                        last.then_inc(acc_copied, 1)

                def tile_of(k):
                    if isinstance(k, int):
                        return k // 2
                    return state["tile"]

                def quad(u, first, last):
                    if first:
                        state["u"] = 0
                        first_terms(0, 0)
                    for kap in range(RING):
                        k = u * RING + kap
                        state["u"] = u
                        have = not (first and kap == 0)
                        copy_samples(k, kap)
                        exps(k, kap)
                        if have:
                            state["tile"] = u * 2 + (kap - 1) // 2
                            copy_acc(k - 1, (kap - 1) % RING)
                        if not (last and kap == RING - 1):
                            nxt = (kap + 1) % RING
                            state["u"] = u + 1 if kap == RING - 1 else u
                            first_terms(k + 1, nxt)
                        if turn:
                            turn_chunk((b + 1) * NPAIR + TPAIRS + u * 2 + kap // 2, kap % 2)

                quads(nc.scalar, quad)
                copy_acc(NHALF - 1, RING - 1)

            def finish(b, attend, query, turn):
                c = b + 1

                def root(j):
                    def run_():
                        act.wait_ge(var_ready, b * 3 + j + 1)
                        fn(std[:], var[:], ACT.Sqrt).then_inc(std_ready, 1)
                    return run_

                def s_xaT():
                    for i in range(4):
                        act.wait_ge(xaT_done, b * 4 + i + 1)
                        fn(xaT[:, i // 2, (i % 2) * TC:(i % 2 + 1) * TC], banks("xaT", i), ACT.Copy).then_inc(xaT_copied, 1)

                def s_qin():
                    act.wait_ge(acc_done, c * (2 * NHALF))
                    for g in range(NT):
                        act.wait_ge(gathered[g], (c * (NT + 1) + 1) * 32)
                        a0 = CONST_COLS["qweight"][0] + 4 * g
                        fn(sq[:, g, :], xg[:, g, 0, 0:C], ACT.Copy, scale=K_[:, a0:a0 + 1]).then_inc(first_term, 1)

                def s_qproj():
                    for i in range(4):
                        act.wait_ge(queT_done, c * 4 + i + 1)
                        fn(queT[:, i // 2, (i % 2) * TC:(i % 2 + 1) * TC], banks("queT", i), ACT.Copy).then_inc(queT_copied, 1)

                def s_qkv():
                    for h in range(CH):
                        act.wait_ge(kmax_ready, b * 2 + h + 1)
                        if h == 0:
                            act.wait_ge(xnT_done, b * 4 + 4)
                        for c2 in range(NC2):
                            fn(ekT[:, h, c2 * TC:(c2 + 1) * TC], banks("k", h * 2 + c2), ACT.Exp, bias=knmax[:, h:h + 1],
                               accum_out=ksum[:, h, c2:c2 + 1]).then_inc(k_exped, 1)
                    for i in range(4):
                        act.wait_ge(q_done, b * 4 + i + 1)
                        fn(qT[:, i // 2, (i % 2) * TC:(i % 2 + 1) * TC], banks("q", i), ACT.Copy).then_inc(q_copied, 1)

                def s_qhidden():
                    act.wait_ge(qvar_ready, c + 1)
                    fn(qsum[:, 3, :], qsum[:, 2, :], ACT.Sqrt).then_inc(qstd_ready, 1)
                    act.wait_ge(qh_normed, c + 1)
                    fn(qo2, qo, ACT.Gelu_apprx_tanh).then_inc(qh_ready, 1)
                    for i in range(2):
                        act.wait_ge(qhT_done, c * 2 + i + 1)
                        fn(qhT[:, i * TC:(i + 1) * TC], banks("qhT", i)[0:FO, :], ACT.Copy).then_inc(qhT_copied, 1)

                def s_xnT():
                    for i in range(4):
                        act.wait_ge(xnT_done, b * 4 + i + 1)
                        fn(xnT[:, i // 2, (i % 2) * TC:(i % 2 + 1) * TC], banks("xnT", i), ACT.Identity,
                           scale=AG[:, i // 2:i // 2 + 1], bias=AB[:, i // 2:i // 2 + 1]).then_inc(xnT_copied, 1)

                def s_hgate():
                    for i in range(2):
                        act.wait_ge(hg_done, b * 2 + i + 1)
                        fn(hg[:, i * TC:(i + 1) * TC], banks("hg", i)[0:FO, :], ACT.Gelu, bias=BG1).then_inc(hg_copied, 1)

                def s_gate():
                    for i in range(4):
                        act.wait_ge(gate_done, b * 4 + i + 1)
                        fn(xnT[:, i // 2, (i % 2) * TC:(i % 2 + 1) * TC], banks("gate", i), ACT.Sigmoid, bias=BG2[:, i // 2:i // 2 + 1])\
                            .then_inc(gate_copied, 1)

                def s_xfT():
                    for i in range(4):
                        act.wait_ge(xfT_done, b * 4 + i + 1)
                        fn(xaT[:, i // 2, (i % 2) * TC:(i % 2 + 1) * TC], banks("xfT", i), ACT.Copy).then_inc(xfT_copied, 1)

                def s_rank():
                    for i in range(2):
                        act.wait_ge(wrow_done, b * 2 + i + 1)
                        fn(wrow[:, i * TC:(i + 1) * TC], banks("wrow", i), ACT.Copy).then_inc(wrow_copied, 1)

                def s_ffn():
                    for c2 in range(NC2):
                        if c2:
                            act.wait_ge(y_done, b * 4 + 2)
                        for j in range(HID // P):
                            act.wait_ge(hid_done, b * 16 + c2 * 8 + j + 1)
                            fn(hid[:, j, :], banks("hid", c2 * 8 + j), ACT.Gelu_apprx_tanh, bias=B1[:, j:j + 1]).then_inc(hid_copied, 1)

                banks = bank_map(end_stages(attend, query, turn))
                run = {"norm1": root(0), "norm2": root(1), "norm3": root(2), "xaT": s_xaT, "qin": s_qin, "qproj": s_qproj, "qkv": s_qkv,
                       "qhidden": s_qhidden, "xnT": s_xnT, "hgate": s_hgate, "gate": s_gate, "xfT": s_xfT, "rank": s_rank, "ffn": s_ffn}
                n = 0
                for s in end_stages(attend, query, turn):
                    if s == "T":
                        turn_pair(b + 2, n)
                        n += 1
                    elif s in run:
                        run[s]()

            images(nc.scalar, sample, finish)

        @block.vector
        def _(dve):
            v = nc.vector
            ch = Chain(dve, dve_step)
            dve.sem_inc(sampled, GT)
            dve.wait_ge(loaded, 16 * (14 + 8 + 3))
            wk_raw = qkT[:].rearrange("p a h q n -> p a (h q n)")[:, :, 0:C]
            a0 = CONST_COLS["head4"][0]
            for n in range(NH):
                ch.step(v.tensor_scalar(WKP[:, n, :], wk_raw[:, n // 4, :], K_[:, a0 + n % 4:a0 + n % 4 + 1], None, ALU.mult))
            ch.step(v.tensor_copy(same_q[:], const("same_q")))
            ch.step(v.tensor_copy(far_q[:], const("far_q")))
            ch.step(v.memset(base[:], 0.0))
            v.tensor_copy(qidx[:], const("qindex").rearrange("p (t r) -> p t r", r=2)).then_inc(qidx_ready, 1)
            ch.link(v.memset(xg[:], 0.0))
            v.memset(cnt[:], 0.0).then_inc(ready0, 1)
            dve.wait_ge(ready0, 1)
            ch.clear()

            def turn_chunk(pair, i):
                dve.wait_ge(rows_turned, pair * 4 + 2 * i + 2)
                dve.wait_ge(rows_stored[i], pair * 16)
                v.tensor_copy(xrow[i][:, 2:4, :].rearrange("p r c -> p (r c)"), rows_bank[1][:]).then_inc(rows_dve, 1)

            def turn_pair(image, jj):
                for i in range(2):
                    turn_chunk(image * NPAIR + jj, i)

            with v.Fori(0, NPAIR) as jj:
                turn_pair(0, jj)

            def terms(groups, count):
                n0 = ch.n
                for k in range(1, 4):
                    for i, (dst, slot, w) in enumerate(groups):
                        if k == 1:
                            dve.wait_ge(first_term, count + i + 1)
                        elif k == 2:
                            ch.wait(n0 + i + 1)
                        else:
                            ch.wait(n0 + len(groups) + i + 1)
                        ins = v.scalar_tensor_tensor(dst, xg[:, slot, k // 2, (k % 2) * C:(k % 2 + 1) * C], w(k), dst, ALU.mult, ALU.add)
                        if k < 3:
                            ch.step(ins)
                        else:
                            ins.then_inc(sampled, 1)

            def sample(b, turn):
                def interp(k, kap, pr):
                    gs = []
                    for g in (2 * pr, 2 * pr + 1):
                        gs.append((smp[:, kap, g, :], (kap * HG + g) % GT, lambda j, g=g: wgt[:, j, bass.ds(k * HG + g, 1)]))
                    terms(gs, b * (NT + NG) + NT + k * HG + 2 * pr)

                def copy_qk(k, kap):
                    hf = kap % 2
                    if not isinstance(k, int) or k >= 2:
                        dve.wait_ge(scores_done, b * NHALF + k - 1)
                    for h in range(CH):
                        dve.wait_ge(qk_done, b * (2 * NHALF) + k * 2 + h + 1)
                        v.tensor_copy(qkT[:, hf, h, :, :].rearrange("p q n -> p n q"),
                                      work_bank[h][:].rearrange("p (n q) -> p n q", n=NH)).then_inc(qk_copied, 1)

                def copy_probs(k, kap):
                    dve.wait_ge(probT_done, b * NHALF + k + 1)
                    if not isinstance(k, int) or k >= 2:
                        dve.wait_ge(acc_done, b * (2 * NHALF) + k * 2 - 2)
                    v.tensor_copy(probs[:, 1, kap % 2, :, :].rearrange("p g n -> p (g n)"), probT_bank[:]).then_inc(probT_copied, 1)

                def maxes(k, kap):
                    hf = kap % 2
                    dve.wait_ge(scores_done, b * NHALF + k + 1)
                    ch.link(v.reduce_max(smax[:, hf, :], score_bank[:].rearrange("p (g n) -> p g n", g=HG), AX.X))
                    v.tensor_scalar(nmax[:, hf, :], smax[:, hf, :], -SCALE, None, ALU.mult).then_inc(max_ready, 1)

                def normalise(k, kap):
                    hf = kap % 2
                    dve.wait_ge(exp_done, b * NHALF + k + 1)
                    ch.link(v.reciprocal(srec[:, hf, :], ssum[:, hf, :]))
                    pv = probs[:, 0, hf, :, :]
                    v.tensor_tensor(pv, pv, srec[:, hf, :].rearrange("p (g o) -> p g o", o=1).broadcast_to([P, HG, P]), ALU.mult)\
                        .then_inc(probs_ready, 1)

                def copy_tokens(t):
                    dve.wait_ge(tok_done, b * NT + t + 1)
                    v.tensor_copy(hbuf[:, t, :], work_bank[0][:, 0:C]).then_inc(tok_copied, 1)

                def quad(u, first, last):
                    if first:
                        dve.wait_ge(out_stored, b * 16)
                        interp(0, 0, 0)
                        interp(0, 0, 1)
                    for kap in range(RING):
                        k = u * RING + kap
                        have = not (first and kap == 0)
                        more = not (last and kap == RING - 1)
                        nxt = (kap + 1) % RING
                        copy_qk(k, kap)
                        if have:
                            copy_probs(k - 1, (kap - 1) % RING)
                        maxes(k, kap)
                        if more:
                            interp(k + 1, nxt, 0)
                        if more:
                            interp(k + 1, nxt, 1)
                        normalise(k, kap)
                        if turn:
                            turn_chunk((b + 1) * NPAIR + TPAIRS + u * 2 + kap // 2, kap % 2)
                        if have and kap % 2 == 0:
                            copy_tokens(u * 2 + kap // 2 - 1)
                    ch.clear()

                quads(v, quad)
                copy_probs(NHALF - 1, RING - 1)
                copy_tokens(NT - 1)

            def finish(b, attend, query, turn):
                c = b + 1
                banks = bank_map(end_stages(attend, query, turn))

                def norm(j, src, ready, prior, guard=None):
                    def run_():
                        dve.wait_ge(*prior())
                        for t in range(NT):
                            ch.step(v.bn_stats(stats[:, t, :], src[:, t, :]))
                        ch.wait()
                        for t in range(NT):
                            ch.step(v.bn_aggr(mv[:, t, :], stats[:, t, :]))
                        ch.wait()
                        v.tensor_scalar(var[:], mv[:, :, 1], EPS, None, ALU.add).then_inc(var_ready, 1)
                        dve.wait_ge(std_ready, b * 3 + j + 1)
                        if guard:
                            dve.wait_ge(*guard())
                        ch.link(v.reciprocal(std[:], std[:]))
                        for t in range(NT):
                            v.tensor_scalar(xa[:, t, :], src[:, t, :], mv[:, t, 0:1], std[:, t:t + 1], ALU.subtract, ALU.mult)\
                                .then_inc(ready, 1)
                    return run_

                def s_qin():
                    for g in range(0, NT, 2):
                        gs = []
                        for i in range(2):
                            a0 = CONST_COLS["qweight"][0] + 4 * (g + i)
                            gs.append((sq[:, g + i, :], g + i, lambda j, a0=a0: K_[:, a0 + j:a0 + j + 1]))
                        terms(gs, c * (NT + NG) + g)

                def s_qfT():
                    dve.wait_ge(tok_done, c * NT)
                    for i in range(4):
                        dve.wait_ge(qfT_done, c * 4 + i + 1)
                        v.tensor_copy(qfT[:, i // 2, (i % 2) * TC:(i % 2 + 1) * TC], banks("qfT", i)).then_inc(qfT_copied, 1)

                def s_qproj():
                    dve.wait_ge(o1_done, c + 1)
                    wide = [P, NT, FO]

                    def over_tiles(r):
                        return r.rearrange("p (o f) -> p o f", o=1).broadcast_to(wide)

                    def over_features(r):
                        return r.rearrange("p (t o) -> p t o", o=1).broadcast_to(wide)

                    v.tensor_tensor(qo, banks("o1", 0).rearrange("p (t f) -> p t f", t=NT), over_tiles(BO1), ALU.add).then_inc(o1_copied, 1)
                    dve.wait_ge(o1_copied, c + 1)
                    ch.link(v.reduce_sum(qsum[:, 0, :], qo, AX.X))
                    ch.link(v.tensor_scalar(qsum[:, 1, :], qsum[:, 0, :], 1.0 / FO, None, ALU.mult))
                    ch.link(v.tensor_tensor(qo, qo, over_features(qsum[:, 1, :]), ALU.subtract))
                    ch.link(v.tensor_tensor(qo2, qo, qo, ALU.mult))
                    ch.link(v.reduce_sum(qsum[:, 0, :], qo2, AX.X))
                    v.tensor_scalar(qsum[:, 2, :], qsum[:, 0, :], 1.0 / FO, EPS, ALU.mult, ALU.add).then_inc(qvar_ready, 1)

                def s_qkv():
                    for h in range(CH):
                        dve.wait_ge(k_done, b * 4 + h * 2 + 2)
                        for c2 in range(NC2):
                            ch.step(v.reduce_max(kmax[:, h, c2:c2 + 1], banks("k", h * 2 + c2), AX.X))
                        ch.wait()
                        ch.link(v.tensor_tensor(knmax[:, h:h + 1], kmax[:, h, 0:1], kmax[:, h, 1:2], ALU.max))
                        v.tensor_scalar(knmax[:, h:h + 1], knmax[:, h:h + 1], -1.0, None, ALU.mult).then_inc(kmax_ready, 1)
                    for i in range(4):
                        dve.wait_ge(v_done, b * 4 + i + 1)
                        v.tensor_copy(vtok[:, 2 * i:2 * i + 2, :].rearrange("p t c -> p (t c)"), banks("v", i)).then_inc(v_copied, 1)

                def s_qhidden():
                    wide = [P, NT, FO]

                    def over_tiles(r):
                        return r.rearrange("p (o f) -> p o f", o=1).broadcast_to(wide)

                    dve.wait_ge(qstd_ready, c + 1)
                    ch.link(v.reciprocal(qsum[:, 3, :], qsum[:, 3, :]))
                    ch.link(v.tensor_tensor(qo, qo, qsum[:, 3, :].rearrange("p (t o) -> p t o", o=1).broadcast_to(wide), ALU.mult))
                    ch.link(v.tensor_tensor(qo, qo, over_tiles(OG), ALU.mult))
                    v.tensor_tensor(qo, qo, over_tiles(OB), ALU.add).then_inc(qh_normed, 1)

                def s_ek():
                    for i in range(4):
                        dve.wait_ge(ek_done, b * 4 + i + 1)
                        v.tensor_copy(ektok[:, 2 * i:2 * i + 2, :].rearrange("p t c -> p (t c)"), banks("ek", i)).then_inc(ek_copied, 1)

                def s_qoff():
                    dve.wait_ge(off_done, c + 1)
                    v.tensor_tensor(qoff[:].rearrange("p t n a -> p t (n a)"), banks("off", 0)[:, 0:NT * 2 * NH].rearrange("p (t m) -> p t m", t=NT),
                                    BO2.rearrange("p (o m) -> p o m", o=1).broadcast_to([P, NT, 2 * NH]), ALU.add).then_inc(off_copied, 1)
                    dve.wait_ge(off_copied, c + 1)
                    ch.link(v.tensor_scalar(qoff[:].rearrange("p t n a -> p (t n a)"), qoff[:].rearrange("p t n a -> p (t n a)"),
                                            OFFSET_SCALE, None, ALU.mult))
                    own = const("own16").rearrange("p (q n) -> p q n", n=NH)
                    for a in range(2):
                        for t in range(NT):
                            dst = spread[:, a, t, :].rearrange("p (q n) -> p q n", n=NH)
                            src = qoff[:, t:t + 1, :, a].broadcast_to([P, GQ, NH])
                            ins = v.tensor_tensor(dst, src, own, ALU.mult)
                            if a == 1 and t == NT - 1:
                                ins.then_inc(spread_ready, 1)
                            else:
                                ch.step(ins)

                def s_ctx():
                    dve.wait_ge(k_exped, b * 4 + 4)
                    ch.link(v.tensor_tensor(krec[:], ksum[:, :, 0], ksum[:, :, 1], ALU.add))
                    ch.link(v.reciprocal(krec[:], krec[:]))
                    dve.wait_ge(ctx_done, b + 1)
                    for h in range(CH):
                        ins = v.scalar_tensor_tensor(ctxm[:, h, :], banks("ctx", 0)[:, h * P:(h + 1) * P], krec[:, h:h + 1], const("heads"),
                                                     ALU.mult, ALU.mult)
                        ins.then_inc(ctx_copied, 1) if h else ch.step(ins)

                def s_qpoints():
                    dve.wait_ge(pts_done, c + 1)
                    refs = const("refs").rearrange("p (a g) -> p a g", a=2)
                    v.scalar_tensor_tensor(pos[:], banks("pts", 0)[:, 0:2 * NG].rearrange("p (a g) -> p a g", a=2),
                                           2.0 / (W - 1), refs, ALU.mult, ALU.add).then_inc(pts_copied, 1)
                    dve.wait_ge(pts_copied, c + 1)
                    ch.link(v.tensor_scalar(pos[:], pos[:], 1.0, 0.5, ALU.add, ALU.mult))
                    ch.link(v.tensor_scalar(pos[:], pos[:], float(W - 1), 0.0, ALU.mult, ALU.max))
                    ch.link(v.tensor_scalar(pos[:], pos[:], float(W - 1), None, ALU.min))
                    ch.link(v.tensor_copy(posi[:], pos[:]))
                    ch.link(v.tensor_copy(posf[:], posi[:]))
                    ch.link(v.tensor_tensor(gtf[:], posf[:], pos[:], ALU.is_gt))
                    ch.link(v.tensor_tensor(posf[:], posf[:], gtf[:], ALU.subtract))
                    ch.link(v.tensor_scalar(posf[:], posf[:], float(W - 2), 0.0, ALU.min, ALU.max))
                    ch.link(v.tensor_tensor(frac[:, 1], pos[:], posf[:], ALU.subtract))
                    ch.link(v.tensor_scalar(frac[:, 0], frac[:, 1], -1.0, 1.0, ALU.mult, ALU.add))
                    for j in range(4):
                        ch.step(v.tensor_tensor(wgt[:, j, :], frac[:, j % 2, 0, :], frac[:, j // 2, 1, :], ALU.mult))
                    ch.link(v.scalar_tensor_tensor(idxf[:], posf[:, 1, :], float(W), posf[:, 0, :], ALU.mult, ALU.add))
                    ch.link(v.tensor_scalar(idxf[:], idxf[:], base[:], None, ALU.add))
                    dve.wait_ge(idx_copied, c * NT)
                    ch.link(v.tensor_copy(idx_all[:, :, 0], idxf[:]))
                    v.tensor_scalar(idx_all[:, :, 1], idxf[:], float(W), None, ALU.add).then_inc(points_ready, 1)
                    ch.link(v.tensor_scalar(base[:], base[:], float(PX), None, ALU.add))
                    ch.link(v.tensor_scalar(wrap[:], base[:], float(SLOTS * PX), float(-SLOTS * PX), ALU.is_ge, ALU.mult))
                    ch.link(v.tensor_tensor(base[:], base[:], wrap[:], ALU.add))
                    v.tensor_scalar(qidx[:], const("qindex").rearrange("p (t r) -> p t r", r=2), base[:], None, ALU.add).then_inc(qidx_ready, 1)
                    dve.wait_ge(points_ready, c + 1)

                def s_mix():
                    for i in range(4):
                        dve.wait_ge(gate_copied, b * 4 + i + 1)
                        dve.wait_ge(mix_done, b * 4 + i + 1)
                        sl = slice((i % 2) * TC, (i % 2 + 1) * TC)
                        v.tensor_tensor(xaT[:, i // 2, sl], banks("mix", i), xnT[:, i // 2, sl], ALU.mult).then_inc(mix_copied, 1)

                def s_proj():
                    flat = hbuf[:]
                    ch.link(v.tensor_tensor(flat, flat, BPROJ.rearrange("p (o c) -> p o c", o=1).broadcast_to([P, NT, C]), ALU.add))
                    for i in range(4):
                        dve.wait_ge(proj_done, b * 4 + i + 1)
                        hv = hbuf[:, 2 * i:2 * i + 2, :].rearrange("p t c -> p (t c)")
                        v.tensor_tensor(hv, banks("proj", i), hv, ALU.add).then_inc(proj_copied, 1)

                def s_rank():
                    dve.wait_ge(xf_ready, (b + 1) * NT)
                    for t in range(NT):
                        ch.step(v.tensor_tensor_reduce(out=ytmp[:, 0, 0, :], in0=xa[:, t, :], in1=WR, scale=1.0, scalar=0.0, op0=ALU.mult,
                                                       op1=ALU.add, accum_out=wtok[:, t:t + 1]))
                        ch.wait()
                    v.tensor_scalar(wtok[:], wtok[:], BR, None, ALU.add).then_inc(w_ready, 1)
                    ch.link(v.tensor_tensor(hbuf[:], hbuf[:], xa, ALU.add))
                    dve.wait_ge(w_ready, b + 1)
                    dve.wait_ge(wrow_copied, b * 2 + 2)
                    for t in range(NT):
                        wt = wtok[:, t:t + 1]
                        if t:
                            ch.link(v.tensor_scalar(junk[:, 0:t * P], wrow[:, 0:t * P], wt, 0.0, ALU.is_ge, ALU.add, accum_out=cnt[:, 0, t:t + 1]))
                        if t < NT - 1:
                            ch.link(v.tensor_scalar(junk[:, (t + 1) * P:NQ], wrow[:, (t + 1) * P:NQ], wt, 0.0, ALU.is_gt, ALU.add,
                                                    accum_out=cnt[:, 1, t:t + 1]))
                        d = wrow[:, t * P:(t + 1) * P]
                        ch.link(v.scalar_tensor_tensor(junk[:, 0:P], d, wt, const("lower"), ALU.is_ge, ALU.mult, accum_out=cnt[:, 2, t:t + 1]))
                        ch.link(v.scalar_tensor_tensor(junk[:, 0:P], d, wt, const("upper"), ALU.is_gt, ALU.mult, accum_out=cnt[:, 3, t:t + 1]))
                    ch.link(v.reduce_sum(rnk[:], cnt[:].rearrange("p a t -> p t a"), AX.X))
                    ch.link(v.scalar_tensor_tensor(wsel[:], rnk[:], float(KK), wtok[:], ALU.is_lt, ALU.mult))

                def s_ffn():
                    for i in range(4):
                        dve.wait_ge(y_done, b * 4 + i + 1)
                        yt = ytmp[:, i % 2]
                        if i >= 2:
                            dve.wait_ge(y_copied, b * NT + 2 * i - 2)
                        ch.link(v.tensor_tensor(yt, banks("y", i).rearrange("p (t c) -> p t c", t=2),
                                                B2.rearrange("p (o c) -> p o c", o=1).broadcast_to([P, 2, C]), ALU.add))
                        for j in range(2):
                            t = 2 * i + j
                            v.scalar_tensor_tensor(hbuf[:, t, :], yt[:, j, :], wsel[:, t:t + 1], hbuf[:, t, :], ALU.mult, ALU.add)\
                                .then_inc(y_copied, 1)

                run = {"norm1": norm(0, hbuf, xa_ready, lambda: (tok_copied, (b + 1) * NT)),
                       "norm2": norm(1, xa, xn_ready, lambda: (xa_ready, (b + 1) * NT), lambda: (xaT_done, b * 4 + 4)),
                       "norm3": norm(2, hbuf, xf_ready, lambda: (proj_copied, b * 4 + 4), lambda: (ek_done, b * 4 + 4)),
                       "qin": s_qin, "qfT": s_qfT, "qproj": s_qproj, "qkv": s_qkv, "qhidden": s_qhidden, "ek": s_ek, "qoff": s_qoff,
                       "ctx": s_ctx, "qpoints": s_qpoints, "mix": s_mix, "proj": s_proj, "rank": s_rank, "ffn": s_ffn}
                n = 0
                for s in end_stages(attend, query, turn):
                    if s == "T":
                        turn_pair(b + 2, n)
                        n += 1
                    elif s in run:
                        run[s]()
                ch.clear()

            images(v, sample, finish)


def constants():
    import numpy as np

    f = np.float32
    parts = {}
    p = np.arange(P)
    parts["ident"] = np.eye(P, dtype=f)
    parts["own16"] = (p[:, None] % GQ == (p // NH)[None, :]).astype(f)
    parts["group8"] = (p[:, None] // GQ == np.arange(GT)[None, :]).astype(f)
    parts["head4"] = (p[:, None] // DH == np.arange(4)[None, :]).astype(f)
    parts["lower"] = (p[None, :] < p[:, None]).astype(f)
    parts["upper"] = (p[None, :] > p[:, None]).astype(f)
    parts["heads"] = (p[:, None] // DH == p[None, :] // DH).astype(f)
    n = W // DS
    grid = np.linspace(-1.0, 1.0, n).astype(f)
    q = np.arange(NG)[None, :] * GQ + (p // NH)[:, None]
    parts["refs"] = np.concatenate([grid[q % n], grid[q // n]], axis=1)
    at = ((grid + f(1)) * f(0.5) * f(W - 1)).astype(f)
    lo = np.clip(np.floor(at), 0, W - 2).astype(f)
    fr = np.clip(at - lo, 0, 1).astype(f)
    q = np.arange(NT)[None, :] * P + p[:, None]
    xj, yi = q % n, q // n
    wx, wy = fr[xj], fr[yi]
    parts["qweight"] = np.stack([(1 - wx) * (1 - wy), wx * (1 - wy), (1 - wx) * wy, wx * wy], axis=-1).reshape(P, -1)
    top = lo[yi] * W + lo[xj]
    parts["qindex"] = np.stack([top, top + W], axis=-1).reshape(P, -1)
    r = np.arange(P)
    same = np.zeros((P, P), f)
    same[:GQ] = (r[:GQ, None] == (p // NH)[None, :])
    parts["same_q"] = same
    far = np.zeros((P, P), f)
    far[:GQ] = f(FAR) * (1 - same[:GQ])
    parts["far_q"] = far
    return np.ascontiguousarray(np.concatenate([parts[k].astype(f) for k in CONST_COLS], axis=1))


def kernel(**inputs):
    import numpy as np
    import concourse.bacc as bacc
    from concourse.bass_utils import run_bass_kernel_spmd

    def a(name):
        return np.asarray(inputs[name])

    arrays = {"x": a("x"), "consts": constants(), "wq_t": a("L0_tok_W_q").T, "wk": a("L0_tok_W_k"), "wv_t": a("L0_tok_W_v").T,
              "wo1": a("L0_tok_W_o1"), "bo1": a("L0_tok_b_o1"), "og": a("L0_tok_ln_g"), "ob": a("L0_tok_ln_b"), "wo2": a("L0_tok_W_o2"),
              "bo2": a("L0_tok_b_o2"), "wqkv": a("L0_attn_Wqkv"), "wproj": a("L0_attn_Wproj"), "bproj": a("L0_attn_bproj"),
              "ag": a("L0_attn_ln_g"), "ab": a("L0_attn_ln_b"), "wg1": a("L0_attn_Wg1"), "bg1": a("L0_attn_bg1"),
              "wg2": a("L0_attn_Wg2"), "bg2": a("L0_attn_bg2"), "wr": a("L0_ffn_wr").reshape(-1), "br": a("L0_ffn_br"),
              "w1": a("L0_ffn_w1"), "b1": a("L0_ffn_b1"), "w2": a("L0_ffn_w2"), "b2": a("L0_ffn_b2")}
    arrays = {k: np.ascontiguousarray(v) for k, v in arrays.items()}
    nc = bacc.Bacc("TRN2", target_bir_lowering=False, num_devices=1)
    args = [nc.dram_tensor("in_" + k, v.shape, mybir.dt.from_np(v.dtype), kind="ExternalInput").ap() for k, v in arrays.items()]
    out = nc.dram_tensor("out", (B * NQ, C), F32, kind="ExternalOutput").ap()
    build_tower(nc, *args, out)
    r = run_bass_kernel_spmd(nc, [{"in_" + k: v for k, v in arrays.items()}], core_ids=[0])
    return r.results[0]["out"].reshape(B, NQ, C)
```
